# Optimizing a Trainium2 kernel written in Bass

```python
import numpy as np
import jax
import jax.numpy as jnp

def _softmax(x, axis=-1):
    return jax.nn.softmax(x, axis=axis)

def _gelu(x):
    return jax.nn.gelu(x, approximate=True)

def _silu(x):
    return jax.nn.silu(x)

def _sigmoid(x):
    return jax.nn.sigmoid(x)

def _layernorm(x, axis=-1, eps=1e-05):
    m = jnp.mean(x, axis=axis, keepdims=True)
    v = jnp.var(x, axis=axis, keepdims=True)
    return (x - m) / jnp.sqrt(v + eps)

def _scatter_add(tgt, idx, src, axis=0):
    return tgt.at[idx].add(src)

def _segment_sum(src, seg, n):
    return jax.ops.segment_sum(src, seg, n)
kernel_name = 'mk_dlrm_tower_d1_rec_r8_636a32'

def setup_inputs(seed: int=0):
    np.random.seed(seed)
    _w = jnp.asarray

    def _rec_inputs():
        import jax
        import jax.numpy as jnp
        _tk = jax.random.key(seed)
        dense_ctx = jax.random.normal(jax.random.fold_in(_tk, 190), (512, 16), jnp.float32)
        ids = jnp.stack([jax.random.randint(jax.random.fold_in(_tk, 200 + f), (512,), 0, v, jnp.int32) for f, v in enumerate([1250, 12500, 125000, 1000, 1000, 1250, 1250, 1000, 1000, 1250, 1250, 12500, 1000, 1000, 12500, 12500, 1000, 1250, 1250, 1000, 1000, 1250, 12500, 1250, 12500, 1250, 1000])], axis=1)
        tbl_0 = 0.05 * jax.random.normal(jax.random.fold_in(_tk, 500 + 0), (1250, 128), jnp.float32)
        tbl_1 = 0.05 * jax.random.normal(jax.random.fold_in(_tk, 500 + 1), (12500, 128), jnp.float32)
        tbl_2 = 0.05 * jax.random.normal(jax.random.fold_in(_tk, 500 + 2), (125000, 128), jnp.float32)
        tbl_3 = 0.05 * jax.random.normal(jax.random.fold_in(_tk, 500 + 3), (1000, 128), jnp.float32)
        tbl_4 = 0.05 * jax.random.normal(jax.random.fold_in(_tk, 500 + 4), (1000, 128), jnp.float32)
        tbl_5 = 0.05 * jax.random.normal(jax.random.fold_in(_tk, 500 + 5), (1250, 128), jnp.float32)
        tbl_6 = 0.05 * jax.random.normal(jax.random.fold_in(_tk, 500 + 6), (1250, 128), jnp.float32)
        tbl_7 = 0.05 * jax.random.normal(jax.random.fold_in(_tk, 500 + 7), (1000, 128), jnp.float32)
        tbl_8 = 0.05 * jax.random.normal(jax.random.fold_in(_tk, 500 + 8), (1000, 128), jnp.float32)
        tbl_9 = 0.05 * jax.random.normal(jax.random.fold_in(_tk, 500 + 9), (1250, 128), jnp.float32)
        tbl_10 = 0.05 * jax.random.normal(jax.random.fold_in(_tk, 500 + 10), (1250, 128), jnp.float32)
        tbl_11 = 0.05 * jax.random.normal(jax.random.fold_in(_tk, 500 + 11), (12500, 128), jnp.float32)
        tbl_12 = 0.05 * jax.random.normal(jax.random.fold_in(_tk, 500 + 12), (1000, 128), jnp.float32)
        tbl_13 = 0.05 * jax.random.normal(jax.random.fold_in(_tk, 500 + 13), (1000, 128), jnp.float32)
        tbl_14 = 0.05 * jax.random.normal(jax.random.fold_in(_tk, 500 + 14), (12500, 128), jnp.float32)
        tbl_15 = 0.05 * jax.random.normal(jax.random.fold_in(_tk, 500 + 15), (12500, 128), jnp.float32)
        tbl_16 = 0.05 * jax.random.normal(jax.random.fold_in(_tk, 500 + 16), (1000, 128), jnp.float32)
        tbl_17 = 0.05 * jax.random.normal(jax.random.fold_in(_tk, 500 + 17), (1250, 128), jnp.float32)
        tbl_18 = 0.05 * jax.random.normal(jax.random.fold_in(_tk, 500 + 18), (1250, 128), jnp.float32)
        tbl_19 = 0.05 * jax.random.normal(jax.random.fold_in(_tk, 500 + 19), (1000, 128), jnp.float32)
        tbl_20 = 0.05 * jax.random.normal(jax.random.fold_in(_tk, 500 + 20), (1000, 128), jnp.float32)
        tbl_21 = 0.05 * jax.random.normal(jax.random.fold_in(_tk, 500 + 21), (1250, 128), jnp.float32)
        tbl_22 = 0.05 * jax.random.normal(jax.random.fold_in(_tk, 500 + 22), (12500, 128), jnp.float32)
        tbl_23 = 0.05 * jax.random.normal(jax.random.fold_in(_tk, 500 + 23), (1250, 128), jnp.float32)
        tbl_24 = 0.05 * jax.random.normal(jax.random.fold_in(_tk, 500 + 24), (12500, 128), jnp.float32)
        tbl_25 = 0.05 * jax.random.normal(jax.random.fold_in(_tk, 500 + 25), (1250, 128), jnp.float32)
        tbl_26 = 0.05 * jax.random.normal(jax.random.fold_in(_tk, 500 + 26), (1000, 128), jnp.float32)
        _rk = jax.random.fold_in(_tk, 7)
        W_top1 = 0.0521996 * jax.random.normal(jax.random.fold_in(_tk, 801), (367, 512), jnp.float32)
        W_top2 = 0.0441942 * jax.random.normal(jax.random.fold_in(_tk, 802), (512, 256), jnp.float32)
        W_top3 = 0.0625 * jax.random.normal(jax.random.fold_in(_tk, 803), (256, 1), jnp.float32)
        b_top1 = jnp.zeros((512,), jnp.float32)
        b_top2 = jnp.zeros((256,), jnp.float32)
        return (dense_ctx, ids, tbl_0, tbl_1, tbl_2, tbl_3, tbl_4, tbl_5, tbl_6, tbl_7, tbl_8, tbl_9, tbl_10, tbl_11, tbl_12, tbl_13, tbl_14, tbl_15, tbl_16, tbl_17, tbl_18, tbl_19, tbl_20, tbl_21, tbl_22, tbl_23, tbl_24, tbl_25, tbl_26, W_top1, b_top1, W_top2, b_top2, W_top3)
    dense_ctx, ids, tbl_0, tbl_1, tbl_2, tbl_3, tbl_4, tbl_5, tbl_6, tbl_7, tbl_8, tbl_9, tbl_10, tbl_11, tbl_12, tbl_13, tbl_14, tbl_15, tbl_16, tbl_17, tbl_18, tbl_19, tbl_20, tbl_21, tbl_22, tbl_23, tbl_24, tbl_25, tbl_26, W_top1, b_top1, W_top2, b_top2, W_top3 = _rec_inputs()

    def _L0_rec_setup():
        import jax, jax.numpy as jnp
        import numpy as np
        NUM_FEATURES = 27
        EMBED_DIM = 128
        BATCH = 4096
        key = jax.random.key(seed)
        inputs = jax.random.normal(key, (BATCH, NUM_FEATURES, EMBED_DIM), dtype=jnp.float32)
        return {'inputs': inputs}
    _L0_rec_all = _L0_rec_setup()
    _L0_rec_in = {k: v for k, v in _L0_rec_all.items() if k in ()}
    del _L0_rec_all
    return {'dense_ctx': dense_ctx, 'ids': ids, 'tbl_0': tbl_0, 'tbl_1': tbl_1, 'tbl_2': tbl_2, 'tbl_3': tbl_3, 'tbl_4': tbl_4, 'tbl_5': tbl_5, 'tbl_6': tbl_6, 'tbl_7': tbl_7, 'tbl_8': tbl_8, 'tbl_9': tbl_9, 'tbl_10': tbl_10, 'tbl_11': tbl_11, 'tbl_12': tbl_12, 'tbl_13': tbl_13, 'tbl_14': tbl_14, 'tbl_15': tbl_15, 'tbl_16': tbl_16, 'tbl_17': tbl_17, 'tbl_18': tbl_18, 'tbl_19': tbl_19, 'tbl_20': tbl_20, 'tbl_21': tbl_21, 'tbl_22': tbl_22, 'tbl_23': tbl_23, 'tbl_24': tbl_24, 'tbl_25': tbl_25, 'tbl_26': tbl_26, 'W_top1': W_top1, 'b_top1': b_top1, 'W_top2': W_top2, 'b_top2': b_top2, 'W_top3': W_top3}

def reference(dense_ctx, ids, tbl_0, tbl_1, tbl_2, tbl_3, tbl_4, tbl_5, tbl_6, tbl_7, tbl_8, tbl_9, tbl_10, tbl_11, tbl_12, tbl_13, tbl_14, tbl_15, tbl_16, tbl_17, tbl_18, tbl_19, tbl_20, tbl_21, tbl_22, tbl_23, tbl_24, tbl_25, tbl_26, W_top1, b_top1, W_top2, b_top2, W_top3):
    import jax
    import jax.numpy as jnp

    def _L0_rec_ref(inputs):
        import jax, jax.numpy as jnp
        import numpy as np
        NUM_FEATURES = 27
        EMBED_DIM = 128
        BATCH = 4096
        interactions = jnp.einsum('bnd,bmd->bnm', inputs, inputs)
        n = inputs.shape[1]
        i, j = jnp.triu_indices(n, k=1)
        return interactions[:, i, j]
    e = jnp.stack([tbl_0[ids[:, 0]], tbl_1[ids[:, 1]], tbl_2[ids[:, 2]], tbl_3[ids[:, 3]], tbl_4[ids[:, 4]], tbl_5[ids[:, 5]], tbl_6[ids[:, 6]], tbl_7[ids[:, 7]], tbl_8[ids[:, 8]], tbl_9[ids[:, 9]], tbl_10[ids[:, 10]], tbl_11[ids[:, 11]], tbl_12[ids[:, 12]], tbl_13[ids[:, 13]], tbl_14[ids[:, 14]], tbl_15[ids[:, 15]], tbl_16[ids[:, 16]], tbl_17[ids[:, 17]], tbl_18[ids[:, 18]], tbl_19[ids[:, 19]], tbl_20[ids[:, 20]], tbl_21[ids[:, 21]], tbl_22[ids[:, 22]], tbl_23[ids[:, 23]], tbl_24[ids[:, 24]], tbl_25[ids[:, 25]], tbl_26[ids[:, 26]]], axis=1)
    z = _L0_rec_ref(e)
    z = z.reshape(z.shape[0], -1)
    h = jnp.concatenate([z, dense_ctx], axis=1)
    h = jnp.maximum(h @ W_top1 + b_top1, 0.0)
    h = jnp.maximum(h @ W_top2 + b_top2, 0.0)
    y = h @ W_top3
    return y

_drawn_inputs = setup_inputs


def setup_inputs(seed=0):
    import zlib

    import numpy as np

    out = dict(_drawn_inputs(seed))
    spreads = {'b_top1': (0.0, 0.1), 'b_top2': (0.0, 0.1)}
    factors = {}
    for name, (base, spread) in spreads.items():
        noise = np.random.default_rng([zlib.crc32(name.encode()), seed]).standard_normal(out[name].shape)
        drawn = base * np.exp(spread * noise) if base else spread * noise
        out[name] = jnp.asarray(drawn.astype(out[name].dtype))
    for name, factor in factors.items():
        out[name] = (out[name] * factor).astype(out[name].dtype)
    return out
```

```python
from contextlib import ExitStack

import concourse.bass as bass
from concourse import mybir

F32 = mybir.dt.float32
I32 = mybir.dt.int32
U32 = mybir.dt.uint32
ALU = mybir.AluOpType
ACT = mybir.ActivationFunctionType

P = 128
QUAD = 32
QUADS = P // QUAD
TGROUP = 4
HALVES = 2


def dlrm_tower(nc, ids, dense, tables, w1, b1, w2, b2, w3, out):
    FEATURES = len(tables)
    CHUNKS = ids.shape[1]
    DROWS, B = dense.shape[1:]
    D = tables[0].shape[1]
    COLS, H1 = w1.shape[1:]
    H2 = w2.shape[2]
    OB1, OB2 = H1 // P, H2 // P
    TGROUPS = -(-FEATURES // TGROUP)
    BLOCKS = P // QUADS
    PERBANK = 512 // P
    REGION = 2 * PERBANK
    REGIONS = BLOCKS // REGION
    assert D == P and B == CHUNKS * P and FEATURES <= QUAD - DROWS and OB1 == 4 and OB2 == 2

    with ExitStack() as ctx:
        def sb(name, shape, dt=F32):
            return ctx.enter_context(nc.sbuf_tensor(name, shape, dt))

        def ps(name, shape):
            return ctx.enter_context(nc.psum_tensor(name, shape, F32))

        def sem(name):
            return ctx.enter_context(nc.semaphore(name))

        idx = sb("idx", [P, CHUNKS, FEATURES], I32)
        rows = sb("rows", [P, CHUNKS, FEATURES, D])
        embT = sb("embT", [P, CHUNKS, BLOCKS, QUADS, QUAD])
        pairs = sb("pairs", [P, COLS, B])
        ident = sb("ident", [P, P])
        w1_sb = sb("w1_sb", [P, COLS, H1])
        w2_sb = sb("w2_sb", [P, OB1, H2])
        w3_sb = sb("w3_sb", [P, OB2])
        b1_sb = sb("b1_sb", [P, OB1])
        b2_sb = sb("b2_sb", [P, OB2])
        h1 = sb("h1", [P, OB1, B])
        h2 = sb("h2", [P, OB2, B])
        y_sb = sb("y_sb", [1, B])

        tp = [ps(f"tp{i}", [P, TGROUP, P]) for i in range(2)]
        gram = [ps(f"gram{i}", [P, REGION, QUADS, QUAD]) for i in range(HALVES)]
        acc = [ps(f"acc{i}", [P, 512]) for i in range(2)]

        s_ids = sem("s_ids")
        s_w1 = sem("s_w1")
        s_small = sem("s_small")
        s_dense = sem("s_dense")
        s_y = sem("s_y")
        s_gath = [[sem(f"s_gath{c}_{q}") for q in range(TGROUPS)] for c in range(CHUNKS)]
        s_zero = sem("s_zero")
        s_padded = sem("s_padded")
        s_cleared = sem("s_cleared")
        s_ident = sem("s_ident")
        s_tp = sem("s_tp")
        s_emb = [sem(f"s_emb{i}") for i in range(2)]
        s_gram = sem("s_gram")
        s_pairs = [sem(f"s_pairs{i}") for i in range(HALVES)]
        s_acc = sem("s_acc")
        s_relu = [sem(f"s_relu{i}") for i in range(2)]

        def relus(c, k):
            each = [OB1 // 2 + OB2 // 2 + 1, OB1 // 2 + OB2 // 2]
            return c * each[k % 2] + k // 2

        def emb_out(eng_copy, n):
            c, q = n // TGROUPS, n % TGROUPS
            t0, t1 = TGROUP * q, min(TGROUP * q + TGROUP, FEATURES)
            return eng_copy(embT[:, c, :, :, t0:t1].rearrange("d g s t -> d s g t"),
                            tp[n % 2][:, 0:t1 - t0, :].rearrange("d t (s g) -> d s g t", s=QUADS))

        def pairs_out(eng_copy, n):
            c, h = n // REGIONS, n % REGIONS
            for s in range(QUADS):
                for j in range(QUADS):
                    b0 = c * P + s * BLOCKS + h * REGION
                    src = gram[n % HALVES][QUAD * s:QUAD * s + FEATURES, :, s, COLS * j:COLS * (j + 1)]
                    last = eng_copy(pairs[QUAD * j:QUAD * j + FEATURES, :, b0:b0 + REGION],
                                    src.rearrange("p g r -> p r g"))
            return last

        block = ctx.enter_context(nc.Block())

        USES = OB1 + OB2 + 1

        @block.sync
        def _(sp):
            sp.dma_start(idx[:, :, :], ids).then_inc(s_ids, 16)
            sp.dma_start(w1_sb[:, :, :], w1).then_inc(s_w1, 16)
            sp.dma_start(w2_sb[:, :, :], w2).then_inc(s_small, 16)
            sp.dma_start(w3_sb[:, :], w3).then_inc(s_small, 16)
            sp.dma_start(b1_sb[:, :], b1).then_inc(s_small, 16)
            sp.dma_start(b2_sb[:, :], b2).then_inc(s_small, 16)
            sp.wait_ge(s_cleared, 1)
            for j in range(QUADS):
                top = QUAD * (j + 1)
                sp.dma_start(pairs[top - DROWS:top, 0, :], dense[j]).then_inc(s_dense, 16)
            for c in range(CHUNKS):
                sp.wait_ge(s_relu[0], relus(c + 1, 0))
                sp.dma_start(out[c], y_sb[0:1, c * P:(c + 1) * P]).then_inc(s_y, 16)
            sp.wait_ge(s_y, 16 * CHUNKS)

        @block.gpsimd
        def _(pool):
            nc.gpsimd.memset(ident[:, :], 0.0).then_inc(s_zero, 1)
            pool.wait_ge(s_zero, 1)
            nc.gpsimd.affine_select(out=ident[:, :], in_=ident[:, :], compare_op=ALU.not_equal, fill=1.0,
                                    base=0, pattern=[[-1, P]], channel_multiplier=1).then_inc(s_ident, 1)
            pool.wait_ge(s_ids, 16)
            for c in range(CHUNKS):
                for t in range(FEATURES):
                    pool.indirect_dma_start(
                        rows[:, c, t, :], None, tables[t],
                        bass.IndirectOffsetOnAxis(ap=idx[:, c, t:t + 1].bitcast(U32), axis=0),
                    ).then_inc(s_gath[c][t // TGROUP], 16)

        @block.tensor
        def _(pe):
            pe.wait_ge(s_ident, 1)
            for c in range(CHUNKS):
                for q in range(TGROUPS):
                    n = c * TGROUPS + q
                    t0, t1 = TGROUP * q, min(TGROUP * q + TGROUP, FEATURES)
                    pe.wait_ge(s_gath[c][q], 16 * (t1 - t0))
                    if n >= 2:
                        pe.wait_ge(s_emb[n % 2], n // 2)
                    for t in range(t0, t1):
                        last = nc.tensor.transpose(tp[n % 2][:, t - t0, :], rows[:, c, t, :], ident[:, :])
                    last.then_inc(s_tp, 1)
                pe.wait_ge(s_emb[0], -(-(c + 1) * TGROUPS // 2))
                pe.wait_ge(s_emb[1], (c + 1) * TGROUPS // 2)
                if c == 0:
                    pe.wait_ge(s_padded, 1)
                for h in range(REGIONS):
                    n = c * REGIONS + h
                    if n >= HALVES:
                        pe.wait_ge(s_pairs[n % HALVES], n // HALVES)
                    for i in range(REGION):
                        four = embT[:, c, h * REGION + i, :, :].rearrange("d s n -> d (s n)")
                        last = nc.tensor.matmul(gram[n % HALVES][:, i, :, :].rearrange("p s n -> p (s n)"), four, four, start=True, stop=True)
                    last.then_inc(s_gram, 1)
                for half in range(HALVES):
                    pe.wait_ge(s_pairs[half], (c + 1) * REGIONS // HALVES)
                if c == 0:
                    pe.wait_ge(s_w1, 16)
                    pe.wait_ge(s_small, 64)
                    pe.wait_ge(s_dense, 16 * QUADS)
                bs = slice(c * P, (c + 1) * P)
                for o in range(OB1):
                    if c > 0 or o >= 2:
                        pe.wait_ge(s_relu[o % 2], relus(c, o))
                    for r in range(COLS):
                        last = nc.tensor.matmul(acc[o % 2][:, 0:P], w1_sb[:, r, o * P:(o + 1) * P],
                                                pairs[:, r, bs], start=(r == 0), stop=(r == COLS - 1))
                    last.then_inc(s_acc, 1)
                for o in range(OB2):
                    for i in range(OB1):
                        pe.wait_ge(s_relu[i % 2], relus(c, OB1 + i % 2))
                        last = nc.tensor.matmul(acc[o % 2][:, 0:P], w2_sb[:, i, o * P:(o + 1) * P],
                                                h1[:, i, bs], start=(i == 0), stop=(i == OB1 - 1))
                    last.then_inc(s_acc, 1)
                for i in range(OB2):
                    pe.wait_ge(s_relu[i], relus(c, OB1 + OB2 + i))
                    last = nc.tensor.matmul(acc[0][0:1, 0:P], w3_sb[:, i:i + 1], h2[:, i, bs],
                                            start=(i == 0), stop=(i == OB2 - 1))
                last.then_inc(s_acc, 1)

        @block.vector
        def _(dve):
            nc.vector.memset(pairs[:, :, :], 0.0).then_inc(s_cleared, 1)
            nc.vector.memset(embT[:, :, :, :, FEATURES:QUAD].rearrange("d c g s n -> d (c g s) n"), 0.0).then_inc(s_padded, 1)
            for c in range(CHUNKS):
                for q in range(TGROUPS):
                    n = c * TGROUPS + q
                    if n % 2 == 0:
                        dve.wait_ge(s_tp, n + 1)
                        emb_out(nc.vector.tensor_copy, n).then_inc(s_emb[0], 1)
                if c == 0:
                    dve.wait_ge(s_cleared, 1)
                for h in range(0, REGIONS, 2):
                    n = c * REGIONS + h
                    dve.wait_ge(s_gram, n + 1)
                    pairs_out(nc.vector.tensor_copy, n).then_inc(s_pairs[0], 1)
                k = c * USES
                bs = slice(c * P, (c + 1) * P)
                if c == 0:
                    dve.wait_ge(s_small, 64)
                for o in range(0, OB1, 2):
                    dve.wait_ge(s_acc, k + o + 1)
                    nc.vector.tensor_scalar(h1[:, o, bs], acc[0][:, 0:P], b1_sb[:, o:o + 1], 0.0,
                                            ALU.add, ALU.max).then_inc(s_relu[0], 1)
                dve.wait_ge(s_acc, k + OB1 + 1)
                nc.vector.tensor_scalar(h2[:, 0, bs], acc[0][:, 0:P], b2_sb[:, 0:1], 0.0,
                                        ALU.add, ALU.max).then_inc(s_relu[0], 1)
                dve.wait_ge(s_acc, k + OB1 + OB2 + 1)
                nc.vector.tensor_copy(y_sb[0:1, bs], acc[0][0:1, 0:P]).then_inc(s_relu[0], 1)

        @block.scalar
        def _(act):
            for c in range(CHUNKS):
                for q in range(TGROUPS):
                    n = c * TGROUPS + q
                    if n % 2 == 1:
                        act.wait_ge(s_tp, n + 1)
                        emb_out(nc.scalar.copy, n).then_inc(s_emb[1], 1)
                if c == 0:
                    act.wait_ge(s_cleared, 1)
                for h in range(1, REGIONS, 2):
                    n = c * REGIONS + h
                    act.wait_ge(s_gram, n + 1)
                    pairs_out(nc.scalar.copy, n).then_inc(s_pairs[1], 1)
                k = c * USES
                bs = slice(c * P, (c + 1) * P)
                if c == 0:
                    act.wait_ge(s_small, 64)
                for o in range(1, OB1, 2):
                    act.wait_ge(s_acc, k + o + 1)
                    nc.scalar.activation(h1[:, o, bs], acc[1][:, 0:P], ACT.Relu,
                                         bias=b1_sb[:, o:o + 1]).then_inc(s_relu[1], 1)
                act.wait_ge(s_acc, k + OB1 + OB2)
                nc.scalar.activation(h2[:, 1, bs], acc[1][:, 0:P], ACT.Relu,
                                     bias=b2_sb[:, 1:2]).then_inc(s_relu[1], 1)


def kernel(**inputs):
    import numpy as np
    import concourse.bacc as bacc
    from concourse.bass_utils import run_bass_kernel_spmd

    ids, dense, w1 = inputs["ids"], inputs["dense_ctx"], inputs["W_top1"]
    B, F = ids.shape
    quads, quad, cols = 4, 32, 7
    h1 = w1.shape[1]
    drows = dense.shape[1] // quads
    placed = np.zeros((quads, quad, cols, h1), w1.dtype)
    at = 0
    for n in range(F):
        for m in range(n + 1, F):
            placed[m // cols, n, m % cols] = w1[at]
            at += 1
    placed[:, quad - drows:, 0] = w1[at:].reshape(quads, drows, h1)

    laid = {"ids": ids.reshape(B // 128, 128, F).transpose(1, 0, 2),
            "dense": dense.T.reshape(quads, drows, B)}
    for t in range(F):
        laid[f"tbl_{t}"] = inputs[f"tbl_{t}"]
    laid["w1"] = placed.reshape(128, cols, h1)
    laid["b1"] = inputs["b_top1"].reshape(-1, 128).T
    laid["w2"] = inputs["W_top2"].reshape(h1 // 128, 128, -1).transpose(1, 0, 2)
    laid["b2"] = inputs["b_top2"].reshape(-1, 128).T
    laid["w3"] = inputs["W_top3"].reshape(-1, 128).T

    nc = bacc.Bacc("TRN2", target_bir_lowering=False, num_devices=1)
    arrays, ap = {}, {}
    for name, a in laid.items():
        a = np.ascontiguousarray(a)
        arrays[f"in_{name}_dram"] = a
        ap[name] = nc.dram_tensor(f"in_{name}_dram", a.shape, mybir.dt.from_np(a.dtype), kind="ExternalInput").ap()
    out = nc.dram_tensor("out_y_dram", (B // 128, 1, 128), F32, kind="ExternalOutput").ap()
    dlrm_tower(nc, ap["ids"], ap["dense"], [ap[f"tbl_{t}"] for t in range(F)],
               ap["w1"], ap["b1"], ap["w2"], ap["b2"], ap["w3"], out)
    r = run_bass_kernel_spmd(nc, [arrays], core_ids=[0])
    return r.results[0]["out_y_dram"].reshape(B, 1)
```

```python
from contextlib import ExitStack

import concourse.bass as bass
from concourse import mybir

F32 = mybir.dt.float32
F32R = mybir.dt.float32r
I32 = mybir.dt.int32
U32 = mybir.dt.uint32
ALU = mybir.AluOpType
ACT = mybir.ActivationFunctionType

P = 128
QUAD = 32
QUADS = P // QUAD
BANK = 512
TGROUP = 4
PICK_ROWS = 8
ROWBUFS = 3
H1_ORDER = (2, 3, 0, 1)
PICKED = (3, 4, 7, 8, 12, 13, 16, 19)


def pair_place(lower, upper):
    return (upper - 1) % QUADS, lower, (upper - 1) // QUADS


def slot_order(features):
    return list(PICKED) + [t for t in range(features) if t not in PICKED]


def dlrm_tower(nc, ids, ids_picked, row_numbers, dense, picked, gathered, w1, b1, w2, b2, w3, out):
    K = len(picked)
    F = K + len(gathered)
    CHUNKS = ids.shape[1]
    DROWS, B = dense.shape[1:]
    D = gathered[0].shape[1]
    TILES, H1 = w1.shape[1:]
    H2 = w2.shape[2]
    OB1, OB2 = H1 // P, H2 // P
    PR = row_numbers.shape[0]
    BLOCKS = P // QUADS
    REGION = 2 * (BANK // P)
    REGIONS = BLOCKS // REGION
    assert D == P and B == CHUNKS * P == BANK and F <= QUAD - DROWS and OB1 == 4 and OB2 == 2
    assert TILES == pair_place(0, F - 1)[2] + 1 and CHUNKS == ROWBUFS + 1

    GROUPS = [(a, min(a + TGROUP, F)) for a in range(K, F, TGROUP)]
    NG = len(GROUPS)

    with ExitStack() as ctx:
        def sb(name, shape, dt=F32):
            return ctx.enter_context(nc.sbuf_tensor(name, shape, dt))

        def ps(name, shape):
            return ctx.enter_context(nc.psum_tensor(name, shape, F32))

        def sem(name):
            return ctx.enter_context(nc.semaphore(name))

        idx = sb("idx", [P, CHUNKS, F - K], I32)
        rows = sb("rows", [P, ROWBUFS, F - K, D])
        embT = sb("embT", [P, CHUNKS, BLOCKS, QUADS, QUAD])
        pairs = sb("pairs", [P, TILES, B])
        ident = sb("ident", [P, P])
        w1_sb = sb("w1_sb", [P, TILES, H1])
        w2_sb = sb("w2_sb", [P, OB1, H2])
        w3_sb = sb("w3_sb", [P, OB2])
        b1_sb = sb("b1_sb", [P, OB1])
        b2_sb = sb("b2_sb", [P, OB2])
        zero = sb("zero", [P, 1])
        h1 = sb("h1", [P, 2, OB1, P])
        h2 = sb("h2", [P, 2, OB2, P])
        y_sb = sb("y_sb", [1, B])
        rownum = sb("rownum", [PR, PICK_ROWS])
        wanted = sb("wanted", [PR, 2, B], I32)
        table = sb("table", [PR, 2, PICK_ROWS, D])
        high = sb("high", [PR, 2, PICK_ROWS, D], F32R)
        low = sb("low", [PR, 2, PICK_ROWS, D], F32R)
        onehot = sb("onehot", [PR, 2, PICK_ROWS, B], F32R)

        tp = [ps(f"tp{i}", [P, TGROUP, P]) for i in range(2)]
        gram = [ps(f"gram{i}", [P, REGION, P]) for i in range(2)]
        acc = [ps(f"acc{i}", [P, BANK]) for i in range(2)]

        s_ids = sem("s_ids")
        s_w1 = sem("s_w1")
        s_small = sem("s_small")
        s_dense = sem("s_dense")
        s_y = sem("s_y")
        s_rownum = sem("s_rownum")
        s_table = [sem(f"s_table{i}") for i in range(2)]
        s_wanted = [sem(f"s_wanted{i}") for i in range(2)]
        s_gath = [[sem(f"s_gath{c}_{q}") for q in range(NG)] for c in range(CHUNKS)]
        s_zeroident = sem("s_zeroident")
        s_zero = sem("s_zero")
        s_ident = sem("s_ident")
        s_padded = sem("s_padded")
        s_cleared = sem("s_cleared")
        s_onehot = sem("s_onehot")
        s_high = sem("s_high")
        s_low = sem("s_low")
        s_pick = sem("s_pick")
        s_pickout = sem("s_pickout")
        s_tp = sem("s_tp")
        s_emb = [sem(f"s_emb{i}") for i in range(2)]
        s_gram = sem("s_gram")
        s_pairs = [sem(f"s_pairs_{e}") for e in ("dve", "act")]
        s_h1 = sem("s_h1")
        s_h1out = [sem(f"s_h1out{i}") for i in range(2)]
        s_h2 = sem("s_h2")
        s_h2out = [sem(f"s_h2out{i}") for i in range(2)]
        s_yacc = sem("s_yacc")
        s_yout = sem("s_yout")

        def h1_bank(o):
            return acc[o][:, 0:P] if o < 2 else gram[o - 2][:, 0, :]

        def emb_out(copy, n):
            a, b = GROUPS[n % NG]
            return copy(embT[:, n // NG, :, :, a:b].rearrange("d g s t -> d s g t"),
                        tp[n % 2][:, 0:b - a, :].rearrange("d t (s g) -> d s g t", s=QUADS))

        def pairs_out(copy, c, h, quadrants):
            for s in quadrants:
                b0 = c * P + s * BLOCKS + h * REGION
                for j in range(QUADS):
                    uppers = range(1 + j, F, QUADS)
                    at = s * (F - 1) + j
                    src = gram[h % 2][QUAD * s:QUAD * s + F, :, at:at + QUADS * (len(uppers) - 1) + 1:QUADS]
                    last = copy(pairs[QUAD * j:QUAD * j + F, 0:len(uppers), b0:b0 + REGION],
                                src.rearrange("p g r -> p r g"))
            return last

        def later_groups(c, o):
            if c + 1 == CHUNKS:
                return []
            after = {2: [0, 1], 3: [2], 0: [3], 1: []}
            after[1 if c + 2 == CHUNKS else 0] += range(4, NG)
            return [NG * (c + 1) + q for q in after[o] if q < NG]

        block = ctx.enter_context(nc.Block())

        @block.sync
        def _(sp):
            def load_picked(i):
                if i >= 2:
                    sp.wait_ge(s_onehot, (i - 1) * PICK_ROWS)
                sp.dma_start(wanted[:, i % 2, :],
                             ids_picked[i:i + 1, :].to_broadcast([PR, B])).then_inc(s_wanted[i % 2], 16)
                if i >= 2:
                    sp.wait_ge(s_low, i - 1)
                rows_of = picked[i].rearrange("(p k) d -> p k d", k=PICK_ROWS)
                cut = PR // 16 * 16
                for a, b in ((0, cut), (cut, PR)):
                    sp.dma_start(table[a:b, i % 2, :, :], rows_of[a:b]).then_inc(s_table[i % 2], 16)

            sp.dma_start(idx[:, :, :], ids).then_inc(s_ids, 16)
            load_picked(0)
            load_picked(1)
            sp.dma_start(w2_sb[:, :, :], w2).then_inc(s_small, 16)
            sp.dma_start(w3_sb[:, :], w3).then_inc(s_small, 16)
            sp.dma_start(b1_sb[:, :], b1).then_inc(s_small, 16)
            sp.dma_start(b2_sb[:, :], b2).then_inc(s_small, 16)
            for i in range(2, K):
                load_picked(i)
            sp.dma_start(w1_sb[:, :, :], w1).then_inc(s_w1, 16)
            sp.wait_ge(s_cleared, 1)
            for j in range(QUADS):
                top = QUAD * (j + 1)
                sp.dma_start(pairs[top - DROWS:top, 0, :], dense[j]).then_inc(s_dense, 16)
            for c in range(CHUNKS):
                sp.wait_ge(s_yout, c + 1)
                sp.dma_start(out[c], y_sb[0:1, c * P:(c + 1) * P]).then_inc(s_y, 16)
            sp.wait_ge(s_y, 16 * CHUNKS)

        @block.gpsimd
        def _(pool):
            nc.gpsimd.memset(ident[:, :], 0.0).then_inc(s_zeroident, 1)
            pool.wait_ge(s_zeroident, 1)
            nc.gpsimd.affine_select(out=ident[:, :], in_=ident[:, :], compare_op=ALU.not_equal, fill=1.0,
                                    base=0, pattern=[[-1, P]], channel_multiplier=1).then_inc(s_ident, 1)
            pool.wait_ge(s_ids, 16)
            for c in range(CHUNKS):
                if c == ROWBUFS:
                    pool.wait_ge(s_tp, NG)
                for q, (a, b) in enumerate(GROUPS):
                    for t in range(a - K, b - K):
                        pool.indirect_dma_start(
                            rows[:, c % ROWBUFS, t, :], None, gathered[t],
                            bass.IndirectOffsetOnAxis(ap=idx[:, c, t:t + 1].bitcast(U32), axis=0),
                        ).then_inc(s_gath[c][q], 16)

        @block.tensor
        def _(pe):
            def pick(i):
                pe.wait_ge(s_high, i + 1)
                if i >= 2:
                    pe.wait_ge(s_pickout, i - 1)
                for k in range(PICK_ROWS):
                    pe.wait_ge(s_onehot, i * PICK_ROWS + k + 1)
                    nc.tensor.matmul(acc[i % 2][:, :], high[:, i % 2, k, :], onehot[:, i % 2, k, :],
                                     start=(k == 0), stop=False)
                pe.wait_ge(s_low, i + 1)
                for k in range(PICK_ROWS):
                    last = nc.tensor.matmul(acc[i % 2][:, :], low[:, i % 2, k, :], onehot[:, i % 2, k, :],
                                            start=False, stop=(k == PICK_ROWS - 1))
                last.then_inc(s_pick, 1)

            def transposes(n):
                c, q = n // NG, n % NG
                a, b = GROUPS[q]
                pe.wait_ge(s_gath[c][q], 16 * (b - a))
                if n >= 2:
                    pe.wait_ge(s_emb[n % 2], n // 2)
                for t in range(a, b):
                    last = nc.tensor.transpose(tp[n % 2][:, t - a, :], rows[:, c % ROWBUFS, t - K, :], ident[:, :])
                last.then_inc(s_tp, 1)

            def gram_region(c, h):
                n = c * REGIONS + h
                if h < 2 and c > 0:
                    pe.wait_ge(s_h1out[h], 2 * c - 1)
                if n >= 2:
                    for e in range(2):
                        pe.wait_ge(s_pairs[e], n - 1)
                for i in range(REGION):
                    four = embT[:, c, h * REGION + i, :, :]
                    last = nc.tensor.matmul(
                        gram[h % 2][:, i, 0:QUADS * (F - 1)].rearrange("p (s n) -> p s n", s=QUADS),
                        four.rearrange("d s n -> d (s n)"), four[:, :, 1:F], start=True, stop=True)
                last.then_inc(s_gram, 1)

            def layer1(c, o):
                for r in range(TILES):
                    last = nc.tensor.matmul(h1_bank(o), w1_sb[:, r, o * P:(o + 1) * P],
                                            pairs[:, r, c * P:(c + 1) * P], start=(r == 0), stop=(r == TILES - 1))
                last.then_inc(s_h1, 1)

            def layer2(c):
                for o in range(OB2):
                    if o == 0:
                        pe.wait_ge(s_h1out[0], 2 * c + 2)
                    for n, i in enumerate(H1_ORDER):
                        if n % 2 == 1 and o == 0:
                            pe.wait_ge(s_h1out[1], 2 * c + n // 2 + 1)
                        last = nc.tensor.matmul(acc[o][:, 0:P], w2_sb[:, i, o * P:(o + 1) * P],
                                                h1[:, c % 2, i, :], start=(n == 0), stop=(n == OB1 - 1))
                    last.then_inc(s_h2, 1)

            def layer3(c):
                for i in range(OB2):
                    pe.wait_ge(s_h2out[i], c + 1)
                    last = nc.tensor.matmul(acc[0][0:1, 0:P], w3_sb[:, i:i + 1], h2[:, c % 2, i, :],
                                            start=(i == 0), stop=(i == OB2 - 1))
                last.then_inc(s_yacc, 1)

            for i in range(K):
                pick(i)
                if i == 0:
                    pe.wait_ge(s_ident, 1)
                if i < NG:
                    transposes(i)
            pe.wait_ge(s_padded, 1)
            pe.wait_ge(s_pickout, K)

            for c in range(CHUNKS):
                for bank in range(2):
                    pe.wait_ge(s_emb[bank], (NG * (c + 1) + 1 - bank) // 2)
                for h in range(REGIONS):
                    gram_region(c, h)
                if c > 0:
                    layer2(c - 1)
                if c == 0:
                    pe.wait_ge(s_w1, 16)
                    pe.wait_ge(s_small, 64)
                    pe.wait_ge(s_dense, 16 * QUADS)
                for e in range(2):
                    pe.wait_ge(s_pairs[e], REGIONS * (c + 1))
                for o in H1_ORDER:
                    if o == 0 and c > 0:
                        pe.wait_ge(s_yout, c)
                    layer1(c, o)
                    for n in later_groups(c, o):
                        transposes(n)
                    if o == 2 and c > 0:
                        layer3(c - 1)
            layer2(CHUNKS - 1)
            layer3(CHUNKS - 1)

        @block.vector
        def _(dve):
            def transposed(n):
                if n % 2 == 0 and n >= NG:
                    dve.wait_ge(s_tp, n + 1)
                    emb_out(nc.vector.tensor_copy, n).then_inc(s_emb[0], 1)

            def h1_block(c, o):
                dve.wait_ge(s_h1, c * OB1 + H1_ORDER.index(o) + 1)
                nc.vector.tensor_scalar(h1[:, c % 2, o, :], h1_bank(o), b1_sb[:, o:o + 1], 0.0,
                                        ALU.add, ALU.max).then_inc(s_h1out[0], 1)

            def h2_block(c):
                dve.wait_ge(s_h2, c * OB2 + 1)
                nc.vector.tensor_scalar(h2[:, c % 2, 0, :], acc[0][:, 0:P], b2_sb[:, 0:1], 0.0,
                                        ALU.add, ALU.max).then_inc(s_h2out[0], 1)

            def y_row(c):
                dve.wait_ge(s_yacc, c + 1)
                nc.vector.tensor_copy(y_sb[0:1, c * P:(c + 1) * P], acc[0][0:1, 0:P]).then_inc(s_yout, 1)

            nc.vector.memset(zero[:, :], 0.0).then_inc(s_zero, 1)
            dve.wait_ge(s_rownum, 16)
            for i in range(K):
                dve.wait_ge(s_wanted[i % 2], 16 * (i // 2 + 1))
                if i >= 2:
                    dve.wait_ge(s_pick, i - 1)
                for k in range(PICK_ROWS):
                    nc.vector.tensor_scalar(onehot[:, i % 2, k, :], wanted[:, i % 2, :], rownum[:, k:k + 1],
                                            None, ALU.is_equal).then_inc(s_onehot, 1)
                dve.wait_ge(s_high, i + 1)
                nc.vector.tensor_tensor(low[:, i % 2], table[:, i % 2], high[:, i % 2].bitcast(F32),
                                        ALU.subtract).then_inc(s_low, 1)
            dve.wait_ge(s_cleared, 1)
            dve.wait_ge(s_small, 64)
            for c in range(CHUNKS):
                for h in range(REGIONS):
                    dve.wait_ge(s_gram, c * REGIONS + h + 1)
                    pairs_out(nc.vector.tensor_copy, c, h, (0, 1)).then_inc(s_pairs[0], 1)
                if c > 0:
                    h2_block(c - 1)
                for o in H1_ORDER:
                    if o % 2 == 0:
                        h1_block(c, o)
                    for n in later_groups(c, o):
                        transposed(n)
                    if o == 2 and c > 0:
                        y_row(c - 1)
            h2_block(CHUNKS - 1)
            y_row(CHUNKS - 1)

        @block.scalar
        def _(act):
            def transposed(n):
                if n % 2 == 1 or n < NG:
                    act.wait_ge(s_tp, n + 1)
                    emb_out(nc.scalar.copy, n).then_inc(s_emb[n % 2], 1)

            def h1_block(c, o):
                act.wait_ge(s_h1, c * OB1 + H1_ORDER.index(o) + 1)
                nc.scalar.activation(h1[:, c % 2, o, :], h1_bank(o), ACT.Relu,
                                     bias=b1_sb[:, o:o + 1]).then_inc(s_h1out[1], 1)

            def h2_block(c):
                act.wait_ge(s_h2, c * OB2 + 2)
                nc.scalar.activation(h2[:, c % 2, 1, :], acc[1][:, 0:P], ACT.Relu,
                                     bias=b2_sb[:, 1:2]).then_inc(s_h2out[1], 1)

            def split(i):
                act.wait_ge(s_table[i % 2], 32 * (i // 2 + 1))
                if i >= 2:
                    act.wait_ge(s_pick, i - 1)
                nc.scalar.copy(high[:, i % 2], table[:, i % 2]).then_inc(s_high, 1)

            act.dma_start(rownum[:, :], row_numbers).then_inc(s_rownum, 16)
            split(0)
            split(1)
            for i in range(K):
                act.wait_ge(s_pick, i + 1)
                nc.scalar.copy(embT[:, :, :, :, i].rearrange("d c g s -> d c s g"),
                               acc[i % 2][:, :].rearrange("d (c s g) -> d c s g", c=CHUNKS, s=QUADS),
                               ).then_inc(s_pickout, 1)
                if i + 2 < K:
                    split(i + 2)
                if i < NG:
                    transposed(i)
                if i == 0:
                    act.wait_ge(s_zero, 1)
                    pads = embT[:, :, :, :, F:QUAD].rearrange("d c g s n -> d (c g s) n")
                    nc.scalar.copy(pads, zero[:, :].unsqueeze(2).to_broadcast(list(pads.shape))).then_inc(s_padded, 1)
                if i == 1:
                    nc.scalar.copy(pairs[:, :, :].rearrange("p r b -> p (r b)"),
                                   zero[:, :].to_broadcast([P, TILES * B])).then_inc(s_cleared, 1)
            act.wait_ge(s_cleared, 1)
            act.wait_ge(s_small, 64)
            for c in range(CHUNKS):
                for h in range(REGIONS):
                    act.wait_ge(s_gram, c * REGIONS + h + 1)
                    pairs_out(nc.scalar.copy, c, h, (2, 3)).then_inc(s_pairs[1], 1)
                if c > 0:
                    h2_block(c - 1)
                for o in H1_ORDER:
                    if o % 2 == 1:
                        h1_block(c, o)
                    for n in later_groups(c, o):
                        transposed(n)
            h2_block(CHUNKS - 1)


def kernel(**inputs):
    import numpy as np
    import concourse.bacc as bacc
    from concourse.bass_utils import run_bass_kernel_spmd

    ids, dense, w1 = inputs["ids"], inputs["dense_ctx"], inputs["W_top1"]
    B, F = ids.shape
    h1 = w1.shape[1]
    drows = dense.shape[1] // QUADS
    order = slot_order(F)
    slot_of = {t: n for n, t in enumerate(order)}
    tiles = pair_place(0, F - 1)[2] + 1
    placed = np.zeros((QUADS, QUAD, tiles, h1), w1.dtype)
    pair = 0
    for t in range(F):
        for u in range(t + 1, F):
            lower, upper = sorted((slot_of[t], slot_of[u]))
            placed[pair_place(lower, upper)] = w1[pair]
            pair += 1
    placed[:, QUAD - drows:, 0] = w1[pair:].reshape(QUADS, drows, h1)

    K = len(PICKED)
    picked_rows = inputs[f"tbl_{PICKED[0]}"].shape[0]
    laid = {
        "ids": ids[:, order[K:]].reshape(B // P, P, F - K).transpose(1, 0, 2),
        "ids_picked": ids[:, order[:K]].T,
        "row_numbers": np.arange(picked_rows, dtype=np.float32).reshape(-1, PICK_ROWS),
        "dense": dense.T.reshape(QUADS, drows, B),
        "w1": placed.reshape(P, tiles, h1),
        "b1": inputs["b_top1"].reshape(-1, P).T,
        "w2": inputs["W_top2"].reshape(h1 // P, P, -1).transpose(1, 0, 2),
        "b2": inputs["b_top2"].reshape(-1, P).T,
        "w3": inputs["W_top3"].reshape(-1, P).T,
    }
    for t in range(F):
        laid[f"tbl_{t}"] = inputs[f"tbl_{t}"]

    nc = bacc.Bacc("TRN2", target_bir_lowering=False, num_devices=1)
    arrays, ap = {}, {}
    for name, a in laid.items():
        a = np.ascontiguousarray(a)
        arrays[f"in_{name}_dram"] = a
        ap[name] = nc.dram_tensor(f"in_{name}_dram", a.shape, mybir.dt.from_np(a.dtype), kind="ExternalInput").ap()
    out = nc.dram_tensor("out_y_dram", (B // P, 1, P), F32, kind="ExternalOutput").ap()
    tables = [ap[f"tbl_{t}"] for t in order]
    dlrm_tower(nc, ap["ids"], ap["ids_picked"], ap["row_numbers"], ap["dense"], tables[:K], tables[K:],
               ap["w1"], ap["b1"], ap["w2"], ap["b2"], ap["w3"], out)
    r = run_bass_kernel_spmd(nc, [arrays], core_ids=[0])
    return r.results[0]["out_y_dram"].reshape(B, 1)
```

```python
from contextlib import ExitStack

import concourse.bass as bass
from concourse import mybir

F32 = mybir.dt.float32
F32R = mybir.dt.float32r
I32 = mybir.dt.int32
U32 = mybir.dt.uint32
ALU = mybir.AluOpType
ACT = mybir.ActivationFunctionType

P = 128
QUAD = 32
QUADS = P // QUAD
BANK = 512
TGROUP = 4
PICK_ROWS = 8
ROWBUFS = 3
WARMUP = 12
TABLEBUFS = 3
TILES = 4
PICKED = (3, 4, 7, 8, 12, 13, 16, 19, 20)


def low_columns(features):
    return features - 1 - QUADS * TILES


def pair_place(lower, upper, features):
    low = low_columns(features)
    if upper > low:
        return (upper - low - 1) % QUADS, lower, (upper - low - 1) // QUADS
    return (upper - 1) // (TILES - 1), moved_row(features) + lower, (upper - 1) % (TILES - 1)


def moved_row(features):
    return features - 1 - QUADS


def slot_order(features):
    return list(PICKED) + [t for t in range(features) if t not in PICKED]


def dlrm_tower(nc, ids, ids_picked, dense, picked, gathered, w1, b1, w2, b2, w3, out):
    K = len(picked)
    F = K + len(gathered)
    CHUNKS = ids.shape[1]
    DROWS, B = dense.shape[1:]
    D = gathered[0].shape[1]
    H1 = w1.shape[2]
    H2 = w2.shape[2]
    OB1, OB2 = H1 // P, H2 // P
    PR = picked[0].shape[0] // PICK_ROWS
    BLOCKS = P // QUADS
    REGION = 2 * (BANK // P)
    REGIONS = BLOCKS // REGION
    assert D == P and B == CHUNKS * P == BANK and F <= QUAD - DROWS and OB1 == 4 and OB2 == 2
    LOW = low_columns(F)
    MOVED = moved_row(F)
    PER_QUADRANT = TILES - 1
    MOVES = -(-LOW // PER_QUADRANT)
    assert 0 < LOW <= QUADS * PER_QUADRANT and MOVED + LOW <= QUAD and CHUNKS == ROWBUFS + 1
    assert w1.shape[1] == TILES

    GROUPS = [(a, min(a + TGROUP, F)) for a in range(K, F, TGROUP)]
    NG = len(GROUPS)
    LASTK = PICK_ROWS - 1

    def low_after(i):
        return 2 if i > 0 else LASTK

    assert K >= TILES and K > NG and NG % 2 == 1

    with ExitStack() as ctx:
        def sb(name, shape, dt=F32):
            return ctx.enter_context(nc.sbuf_tensor(name, shape, dt))

        def ps(name, shape):
            return ctx.enter_context(nc.psum_tensor(name, shape, F32))

        def sem(name):
            return ctx.enter_context(nc.semaphore(name))

        idx = sb("idx", [P, CHUNKS, F - K], I32)
        rows = sb("rows", [P, ROWBUFS, F - K, D])
        embT = sb("embT", [P, CHUNKS, BLOCKS, QUADS, QUAD])
        pairs = sb("pairs", [P, TILES, B])
        stage = sb("stage", [LOW, 2, LOW, P])
        ident = sb("ident", [P, P])
        w1_sb = sb("w1_sb", [P, TILES, H1])
        w2_sb = sb("w2_sb", [P, OB1, H2])
        w3_sb = sb("w3_sb", [P, OB2])
        b1_sb = sb("b1_sb", [P, OB1])
        b2_sb = sb("b2_sb", [P, OB2])
        zero = sb("zero", [P, 1])
        h1 = sb("h1", [P, 2, OB1, P])
        h2 = sb("h2", [P, 2, OB2, P])
        y_sb = sb("y_sb", [1, B])
        rownum = sb("rownum", [PR, PICK_ROWS])
        wanted = sb("wanted", [PR, TABLEBUFS, B], I32)
        table = sb("table", [PR, TABLEBUFS, PICK_ROWS, D])
        high = sb("high", [PR, 2, PICK_ROWS, D], F32R)
        low = sb("low", [PR, 2, PICK_ROWS, D], F32R)
        onehot = sb("onehot", [PR, 2, PICK_ROWS, B], F32R)
        last_negated = sb("last_negated", [PR, 1])
        one = sb("one", [PR, 1])
        off = sb("off", [PR, B])

        tp = [ps(f"tp{i}", [P, TGROUP, P]) for i in range(2)]
        gram = [ps(f"gram{i}", [P, REGION, P]) for i in range(2)]
        acc = [ps(f"acc{i}", [P, BANK]) for i in range(2)]

        s_ids = sem("s_ids")
        s_w1 = sem("s_w1")
        s_small = sem("s_small")
        s_dense = sem("s_dense")
        s_y = sem("s_y")
        s_rownum = sem("s_rownum")
        s_table = [sem(f"s_table{i}") for i in range(TABLEBUFS)]
        s_wanted = [sem(f"s_wanted{i}") for i in range(TABLEBUFS)]
        s_gath = [[sem(f"s_gath{c}_{q}") for q in range(NG)] for c in range(CHUNKS)]
        s_zeroident = sem("s_zeroident")
        s_zero = sem("s_zero")
        s_ident = sem("s_ident")
        s_padded = sem("s_padded")
        s_cleared = sem("s_cleared")
        s_onehot = sem("s_onehot")
        s_lasthot = sem("s_lasthot")
        s_consts = sem("s_consts")
        s_negated = sem("s_negated")
        s_off = sem("s_off")
        s_high = sem("s_high")
        s_low = sem("s_low")
        s_pick = sem("s_pick")
        s_pickout = sem("s_pickout")
        s_tp = sem("s_tp")
        s_emb = [sem(f"s_emb{i}") for i in range(2)]
        s_gram = sem("s_gram")
        s_pairs = [sem(f"s_pairs_{e}") for e in ("dve", "act")]
        s_moved = [sem(f"s_moved{i}") for i in range(2)]
        s_h1 = sem("s_h1")
        s_h1out = [sem(f"s_h1out{i}") for i in range(2)]
        s_h2 = sem("s_h2")
        s_h2out = [sem(f"s_h2out{i}") for i in range(2)]
        s_yacc = sem("s_yacc")
        s_yout = sem("s_yout")

        def h1_bank(o):
            return acc[o][:, 0:P] if o < 2 else gram[o - 2][:, 0, :]

        def emb_out(copy, n):
            a, b = GROUPS[n % NG]
            return copy(embT[:, n // NG, :, :, a:b].rearrange("d g s t -> d s g t"),
                        tp[n % 2][:, 0:b - a, :].rearrange("d t (s g) -> d s g t", s=QUADS))

        def pairs_out(copy, c, h, quadrants):
            for s in quadrants:
                b0 = s * BLOCKS + h * REGION
                rows_of = gram[h % 2][QUAD * s:QUAD * s + F]
                for j in range(QUADS):
                    at = s * (F - 1) + LOW + j
                    copy(pairs[QUAD * j:QUAD * j + F, :, c * P + b0:c * P + b0 + REGION],
                         rows_of[:, :, at:at + QUADS * (TILES - 1) + 1:QUADS].rearrange("p g r -> p r g"))
                last = copy(stage[:, c % 2, :, b0:b0 + REGION],
                            rows_of[0:LOW, :, s * (F - 1):s * (F - 1) + LOW].rearrange("p g r -> p r g"))
            return last

        H1_LAST = (2, 3, 0, 1)

        def h1_order(c):
            if c == CHUNKS - 2:
                return EARLY + tuple(o for o in range(OB1) if o not in EARLY)
            return h2_order(c)

        def h2_order(c):
            return H1_LAST if c == CHUNKS - 1 else tuple(range(OB1))

        def moved_count(c):
            return 16 * MOVES * (c // 2 + 1)

        def h1_done(c, o):
            return c * OB1 + h1_order(c).index(o) + 1

        def h1_left(c, o):
            return 2 * c + h1_order(c).index(o) // 2 + 1

        def h2_bank(c, o):
            return h1_bank(h2_order(c)[o])

        def y_bank(c):
            return acc[0][0:1, 0:P] if c < CHUNKS - 2 else tp[c % 2][0:1, 0, :]

        def groups_after(c, o):
            if c == 0:
                return range(NG + 2 + o, min(NG + 3 + o, 2 * NG))
            if c + 1 == CHUNKS:
                return []
            after = [range(0, 2), range(2, 3), range(3, 4), range(4, NG)][o]
            if c + 2 == CHUNKS:
                after = [range(0, 1), range(1, 2), range(2, 3), range(0)][o]
            return [NG * (c + 1) + q for q in after]

        EARLY = (2, 3)
        LATE = ((CHUNKS * NG - 2, CHUNKS * NG - 1), ())
        assert NG == 5 and NG - 2 <= REGIONS

        block = ctx.enter_context(nc.Block())

        @block.sync
        def _(sp):
            def load_picked(i):
                if i >= TABLEBUFS:
                    sp.wait_ge(s_onehot, (i - TABLEBUFS + 1) * LASTK)
                    sp.wait_ge(s_lasthot, i - TABLEBUFS + 1)
                sp.dma_start(wanted[:, i % TABLEBUFS, :],
                             ids_picked[i:i + 1, :].to_broadcast([PR, B])).then_inc(s_wanted[i % TABLEBUFS], 16)
                if i >= TABLEBUFS:
                    sp.wait_ge(s_low, i - TABLEBUFS + 1)
                rows_of = picked[i].rearrange("(p k) d -> p k d", k=PICK_ROWS)
                cut = PR // 16 * 16
                for a, b in ((0, cut), (cut, PR)):
                    sp.dma_start(table[a:b, i % TABLEBUFS, :, :], rows_of[a:b]).then_inc(s_table[i % TABLEBUFS], 16)

            sp.dma_start(idx[:, :, :], ids).then_inc(s_ids, 16)
            for i in range(TABLEBUFS):
                load_picked(i)
            sp.dma_start(w2_sb[:, :, :], w2).then_inc(s_small, 16)
            sp.dma_start(w3_sb[:, :], w3).then_inc(s_small, 16)
            sp.dma_start(b1_sb[:, :], b1).then_inc(s_small, 16)
            sp.dma_start(b2_sb[:, :], b2).then_inc(s_small, 16)
            for i in range(TABLEBUFS, K):
                load_picked(i)
            sp.dma_start(w1_sb[:, :, :], w1).then_inc(s_w1, 16)
            sp.wait_ge(s_cleared, TILES)
            for j in range(QUADS):
                top = QUAD * (j + 1)
                sp.dma_start(pairs[top - DROWS:top, TILES - 1, :], dense[j]).then_inc(s_dense, 16)

            def store_y(c):
                sp.wait_ge(s_yout, c + 1)
                sp.dma_start(out[c], y_sb[0:1, c * P:(c + 1) * P]).then_inc(s_y, 16)

            for c in range(CHUNKS):
                for e in range(2):
                    sp.wait_ge(s_pairs[e], REGIONS * (c + 1))
                for j in range(MOVES):
                    u0, u1 = PER_QUADRANT * j, min(PER_QUADRANT * (j + 1), LOW)
                    sp.dma_start(pairs[QUAD * j + MOVED:QUAD * j + MOVED + u1, 0:u1 - u0, c * P:(c + 1) * P],
                                 stage[0:u1, c % 2, u0:u1, :]).then_inc(s_moved[c % 2], 16)
                if c > 0:
                    store_y(c - 1)
            store_y(CHUNKS - 1)
            sp.wait_ge(s_y, 16 * CHUNKS)

        @block.gpsimd
        def _(pool):
            nc.gpsimd.iota(rownum[:, :], base=0, pattern=[[1, PICK_ROWS]], channel_multiplier=PICK_ROWS,
                           allow_small_or_imprecise_dtypes=True).then_inc(s_rownum, 1)
            nc.gpsimd.iota(last_negated[:, :], base=-LASTK, pattern=[[0, 1]], channel_multiplier=-PICK_ROWS,
                           allow_small_or_imprecise_dtypes=True).then_inc(s_negated, 1)
            nc.gpsimd.memset(ident[:, :], 0.0).then_inc(s_zeroident, 1)
            pool.wait_ge(s_zeroident, 1)
            nc.gpsimd.affine_select(out=ident[:, :], in_=ident[:, :], compare_op=ALU.not_equal, fill=1.0,
                                    base=0, pattern=[[-1, P]], channel_multiplier=1).then_inc(s_ident, 1)
            pool.wait_ge(s_ids, 16)
            for c in range(CHUNKS):
                if c == ROWBUFS:
                    pool.wait_ge(s_tp, NG)
                for q, (a, b) in enumerate(GROUPS):
                    for t in range(a - K, b - K):
                        pool.indirect_dma_start(
                            rows[:, c % ROWBUFS, t, :], None, gathered[t],
                            bass.IndirectOffsetOnAxis(ap=idx[:, c, t:t + 1].bitcast(U32), axis=0),
                        ).then_inc(s_gath[c][q], 16)

        @block.tensor
        def _(pe):
            def pick(i):
                pe.wait_ge(s_high, i + 1)
                if i >= 2:
                    pe.wait_ge(s_pickout, i - 1)
                early = low_after(i)
                order = (*range(early), LASTK, *range(early, LASTK))
                for n, k in enumerate(order):
                    if k == LASTK:
                        pe.wait_ge(s_lasthot, i + 1)
                    else:
                        pe.wait_ge(s_onehot, i * LASTK + k + 1)
                    nc.tensor.matmul(acc[i % 2][:, :], high[:, i % 2, k, :], onehot[:, i % 2, k, :],
                                     start=(n == 0), stop=False)
                    if n < early:
                        continue
                    if n == early:
                        pe.wait_ge(s_low, i + 1)
                    parts = order[:early + 1] if n == early else (k,)
                    for m in parts:
                        last = nc.tensor.matmul(acc[i % 2][:, :], low[:, i % 2, m, :], onehot[:, i % 2, m, :],
                                                start=False, stop=(n == len(order) - 1 and m == parts[-1]))
                last.then_inc(s_pick, 1)

            def transposes(n):
                c, q = n // NG, n % NG
                a, b = GROUPS[q]
                pe.wait_ge(s_gath[c][q], 16 * (b - a))
                if n >= 2:
                    pe.wait_ge(s_emb[n % 2], n // 2)
                for t in range(a, b):
                    last = nc.tensor.transpose(tp[n % 2][:, t - a, :], rows[:, c % ROWBUFS, t - K, :], ident[:, :])
                last.then_inc(s_tp, 1)

            def gram_region(c, h):
                n = c * REGIONS + h
                if h < 2 and c >= 2:
                    before = c - 1 if c == CHUNKS - 1 else c - 2
                    pe.wait_ge(s_h1out[h], h1_left(before, 2 + h))
                if n >= 2:
                    for e in range(2):
                        pe.wait_ge(s_pairs[e], n - 1)
                for i in range(REGION):
                    four = embT[:, c, h * REGION + i, :, :]
                    last = nc.tensor.matmul(
                        gram[h % 2][:, i, 0:QUADS * (F - 1)].rearrange("p (s n) -> p s n", s=QUADS),
                        four.rearrange("d s n -> d (s n)"), four[:, :, 1:F], start=True, stop=True)
                last.then_inc(s_gram, 1)

            def layer1_tiles(c, o, tiles, begins, ends):
                for n, r in enumerate(tiles):
                    last = nc.tensor.matmul(h1_bank(o), w1_sb[:, r, o * P:(o + 1) * P],
                                            pairs[:, r, c * P:(c + 1) * P], start=(begins and n == 0),
                                            stop=(ends and n == len(tiles) - 1))
                if ends:
                    last.then_inc(s_h1, 1)

            def layer1(c, o):
                layer1_tiles(c, o, range(TILES), True, True)

            def layer2(c):
                order = h2_order(c)
                for i in order:
                    pe.wait_ge(s_h1out[i % 2], h1_left(c, i))
                    for o in range(OB2):
                        if i == order[0] and o == 1:
                            pe.wait_ge(s_h1out[1], h1_left(c, order[1]))
                        last = nc.tensor.matmul(h2_bank(c, o), w2_sb[:, i, o * P:(o + 1) * P],
                                                h1[:, c % 2, i, :], start=(i == order[0]), stop=(i == order[-1]))
                        if i == order[-1]:
                            last.then_inc(s_h2, 1)

            def layer3(c):
                for i in range(OB2):
                    pe.wait_ge(s_h2out[i], c + 1)
                    last = nc.tensor.matmul(y_bank(c), w3_sb[:, i:i + 1], h2[:, c % 2, i, :],
                                            start=(i == 0), stop=(i == OB2 - 1))
                last.then_inc(s_yacc, 1)

            pe.wait_ge(s_ident, 1)
            for _ in range(WARMUP):
                nc.tensor.matmul(acc[1][:, 0:P], ident[:, :], ident[:, :], start=True, stop=True)
            for i in range(K):
                pick(i)
                if 1 <= i <= NG:
                    transposes(i - 1)
            transposes(NG)
            transposes(NG + 1)
            pe.wait_ge(s_padded, 1)
            pe.wait_ge(s_pickout, K)

            for c in range(CHUNKS):
                for bank in range(2):
                    pe.wait_ge(s_emb[bank], (NG * (c + 1) + 1 - bank) // 2)
                for h in range(REGIONS):
                    gram_region(c, h)
                    if h == 0 and 2 <= c < CHUNKS - 1:
                        layer3(c - 2)
                    if c == 0:
                        for n in groups_after(c, h):
                            transposes(n)
                if c == 0:
                    continue
                if c == 1:
                    pe.wait_ge(s_w1, 16)
                    pe.wait_ge(s_small, 64)
                    pe.wait_ge(s_dense, 16 * QUADS)
                pe.wait_ge(s_moved[(c - 1) % 2], moved_count(c - 1))
                for o in h1_order(c - 1):
                    if c == CHUNKS - 1 and o in EARLY:
                        continue
                    if o == 0 and c >= 2:
                        pe.wait_ge(s_yout, c - 1)
                    if o >= 2:
                        for e in range(2):
                            pe.wait_ge(s_pairs[e], REGIONS * c + o + 1)
                    layer1(c - 1, o)
                    for n in groups_after(c, o):
                        transposes(n)
                if c < CHUNKS - 1:
                    layer2(c - 1)
                if c == CHUNKS - 2:
                    pe.wait_ge(s_moved[c % 2], moved_count(c))
                    for o, groups in zip(EARLY, LATE):
                        layer1(c, o)
                        if o == EARLY[0]:
                            layer3(c - 1)
                        for n in groups:
                            transposes(n)
            c = CHUNKS - 1
            for e in range(2):
                pe.wait_ge(s_pairs[e], REGIONS * CHUNKS)
            for o in H1_LAST:
                if o == 0:
                    layer2(c - 1)
                if o < 2:
                    pe.wait_ge(s_h2out[o], c)
                layer1_tiles(c, o, [TILES - 1], True, False)
            layer3(c - 1)
            pe.wait_ge(s_moved[c % 2], moved_count(c))
            for o in H1_LAST:
                layer1_tiles(c, o, range(TILES - 1), False, True)
            layer2(c)
            layer3(c)

        @block.vector
        def _(dve):
            def transposed(n):
                if n == NG or (n % 2 == 0 and n > NG):
                    dve.wait_ge(s_tp, n + 1)
                    emb_out(nc.vector.tensor_copy, n).then_inc(s_emb[n % 2], 1)

            def h1_block(c, o):
                dve.wait_ge(s_h1, h1_done(c, o))
                nc.vector.tensor_scalar(h1[:, c % 2, o, :], h1_bank(o), b1_sb[:, o:o + 1], 0.0,
                                        ALU.add, ALU.max).then_inc(s_h1out[0], 1)

            def h2_block(c):
                dve.wait_ge(s_h2, c * OB2 + 1)
                nc.vector.tensor_scalar(h2[:, c % 2, 0, :], h2_bank(c, 0), b2_sb[:, 0:1], 0.0,
                                        ALU.add, ALU.max).then_inc(s_h2out[0], 1)

            def y_row(c):
                dve.wait_ge(s_yacc, c + 1)
                nc.vector.tensor_copy(y_sb[0:1, c * P:(c + 1) * P], y_bank(c)).then_inc(s_yout, 1)

            nc.vector.memset(zero[:, :], 0.0).then_inc(s_zero, 1)
            nc.vector.memset(one[:, :], 1.0).then_inc(s_consts, 1)
            dve.wait_ge(s_rownum, 1)
            for i in range(K):
                dve.wait_ge(s_wanted[i % TABLEBUFS], 16 * (i // TABLEBUFS + 1))
                if i >= 2:
                    dve.wait_ge(s_pick, i - 1)
                for k in range(LASTK):
                    nc.vector.tensor_scalar(onehot[:, i % 2, k, :], wanted[:, i % TABLEBUFS, :], rownum[:, k:k + 1],
                                            None, ALU.is_equal).then_inc(s_onehot, 1)
                    if k + 1 == low_after(i):
                        dve.wait_ge(s_high, i + 1)
                        nc.vector.tensor_tensor(low[:, i % 2], table[:, i % TABLEBUFS], high[:, i % 2].bitcast(F32),
                                                ALU.subtract).then_inc(s_low, 1)
            transposed(NG)
            transposed(NG + 1)
            dve.wait_ge(s_cleared, TILES)
            dve.wait_ge(s_small, 64)
            for c in range(CHUNKS):
                if c >= 2:
                    if c < CHUNKS - 1:
                        h2_block(c - 2)
                    dve.wait_ge(s_moved[c % 2], moved_count(c - 2))
                for h in range(REGIONS):
                    dve.wait_ge(s_gram, c * REGIONS + h + 1)
                    pairs_out(nc.vector.tensor_copy, c, h, (0, 1)).then_inc(s_pairs[0], 1)
                    if h == 0 and 2 <= c < CHUNKS - 1:
                        y_row(c - 2)
                    if c == 0:
                        for n in groups_after(c, h):
                            transposed(n)
                for o in h1_order(c - 1) if c > 0 else []:
                    if o % 2 == 0 and not (c == CHUNKS - 1 and o in EARLY):
                        h1_block(c - 1, o)
                    for n in groups_after(c, o):
                        transposed(n)
                if c == CHUNKS - 2:
                    h2_block(c - 1)
                    for o, groups in zip(EARLY, LATE):
                        if o % 2 == 0:
                            h1_block(c, o)
                        if o == EARLY[0]:
                            y_row(c - 1)
                        for n in groups:
                            transposed(n)
            c = CHUNKS - 1
            h2_block(c - 1)
            y_row(c - 1)
            h1_block(c, 2)
            h1_block(c, 0)
            h2_block(c)
            y_row(c)

        @block.scalar
        def _(act):
            def transposed(n):
                if n < NG or (n % 2 == 1 and n > NG):
                    act.wait_ge(s_tp, n + 1)
                    emb_out(nc.scalar.copy, n).then_inc(s_emb[n % 2], 1)

            def h1_block(c, o):
                act.wait_ge(s_h1, h1_done(c, o))
                nc.scalar.activation(h1[:, c % 2, o, :], h1_bank(o), ACT.Relu,
                                     bias=b1_sb[:, o:o + 1]).then_inc(s_h1out[1], 1)

            def h2_block(c):
                act.wait_ge(s_h2, c * OB2 + 2)
                nc.scalar.activation(h2[:, c % 2, 1, :], h2_bank(c, 1), ACT.Relu,
                                     bias=b2_sb[:, 1:2]).then_inc(s_h2out[1], 1)

            def split(i):
                act.wait_ge(s_table[i % TABLEBUFS], 32 * (i // TABLEBUFS + 1))
                if i >= 2:
                    act.wait_ge(s_pick, i - 1)
                nc.scalar.copy(high[:, i % 2], table[:, i % TABLEBUFS]).then_inc(s_high, 1)

            def last_onehot(i):
                act.wait_ge(s_wanted[i % TABLEBUFS], 16 * (i // TABLEBUFS + 1))
                if i >= 1:
                    act.wait_ge(s_lasthot, i)
                if i >= 2:
                    act.wait_ge(s_pick, i - 1)
                nc.scalar.activation(off[:, :], wanted[:, i % TABLEBUFS, :], ACT.Abs,
                                     bias=last_negated[:, :]).then_inc(s_off, 1)
                act.wait_ge(s_off, i + 1)
                nc.scalar.activation(onehot[:, i % 2, LASTK, :], off[:, :], ACT.Relu,
                                     bias=one[:, :], scale=-1.0).then_inc(s_lasthot, 1)

            act.wait_ge(s_zero, 1)
            pads = embT[:, :, :, :, F:QUAD].rearrange("d c g s n -> d (c g s) n")
            nc.scalar.copy(pads, zero[:, :].unsqueeze(2).to_broadcast(list(pads.shape))).then_inc(s_padded, 1)
            act.wait_ge(s_negated, 1)
            act.wait_ge(s_consts, 1)
            split(0)
            last_onehot(0)
            split(1)
            last_onehot(1)
            for i in range(K):
                if i < TILES:
                    nc.scalar.copy(pairs[:, i, :], zero[:, :].to_broadcast([P, B])).then_inc(s_cleared, 1)
                act.wait_ge(s_pick, i + 1)
                if i + 2 < K:
                    split(i + 2)
                nc.scalar.copy(embT[:, :, :, :, i].rearrange("d c g s -> d c s g"),
                               acc[i % 2][:, :].rearrange("d (c s g) -> d c s g", c=CHUNKS, s=QUADS),
                               ).then_inc(s_pickout, 1)
                if i + 2 < K:
                    last_onehot(i + 2)
                if 1 <= i <= NG:
                    transposed(i - 1)
            act.wait_ge(s_cleared, TILES)
            act.wait_ge(s_small, 64)
            for c in range(CHUNKS):
                if c >= 2:
                    if c < CHUNKS - 1:
                        h2_block(c - 2)
                    act.wait_ge(s_moved[c % 2], moved_count(c - 2))
                for h in range(REGIONS):
                    act.wait_ge(s_gram, c * REGIONS + h + 1)
                    pairs_out(nc.scalar.copy, c, h, (2, 3)).then_inc(s_pairs[1], 1)
                    if c == 0:
                        for n in groups_after(c, h):
                            transposed(n)
                for o in h1_order(c - 1) if c > 0 else []:
                    if o % 2 == 1 and not (c == CHUNKS - 1 and o in EARLY):
                        h1_block(c - 1, o)
                    for n in groups_after(c, o):
                        transposed(n)
                if c == CHUNKS - 2:
                    h2_block(c - 1)
                    for o, groups in zip(EARLY, LATE):
                        if o % 2 == 1:
                            h1_block(c, o)
                        for n in groups:
                            transposed(n)
            c = CHUNKS - 1
            h2_block(c - 1)
            h1_block(c, 3)
            h1_block(c, 1)
            h2_block(c)


def kernel(**inputs):
    import numpy as np
    import concourse.bacc as bacc
    from concourse.bass_utils import run_bass_kernel_spmd

    ids, dense, w1 = inputs["ids"], inputs["dense_ctx"], inputs["W_top1"]
    B, F = ids.shape
    h1 = w1.shape[1]
    drows = dense.shape[1] // QUADS
    order = slot_order(F)
    slot_of = {t: n for n, t in enumerate(order)}
    placed = np.zeros((QUADS, QUAD, TILES, h1), w1.dtype)
    pair = 0
    for t in range(F):
        for u in range(t + 1, F):
            lower, upper = sorted((slot_of[t], slot_of[u]))
            placed[pair_place(lower, upper, F)] = w1[pair]
            pair += 1
    placed[:, QUAD - drows:, TILES - 1] = w1[pair:].reshape(QUADS, drows, h1)

    K = len(PICKED)
    laid = {
        "ids": ids[:, order[K:]].reshape(B // P, P, F - K).transpose(1, 0, 2),
        "ids_picked": ids[:, order[:K]].T,
        "dense": dense.T.reshape(QUADS, drows, B),
        "w1": placed.reshape(P, TILES, h1),
        "b1": inputs["b_top1"].reshape(-1, P).T,
        "w2": inputs["W_top2"].reshape(h1 // P, P, -1).transpose(1, 0, 2),
        "b2": inputs["b_top2"].reshape(-1, P).T,
        "w3": inputs["W_top3"].reshape(-1, P).T,
    }
    for t in range(F):
        laid[f"tbl_{t}"] = inputs[f"tbl_{t}"]

    nc = bacc.Bacc("TRN2", target_bir_lowering=False, num_devices=1)
    arrays, ap = {}, {}
    for name, a in laid.items():
        a = np.ascontiguousarray(a)
        arrays[f"in_{name}_dram"] = a
        ap[name] = nc.dram_tensor(f"in_{name}_dram", a.shape, mybir.dt.from_np(a.dtype), kind="ExternalInput").ap()
    out = nc.dram_tensor("out_y_dram", (B // P, 1, P), F32, kind="ExternalOutput").ap()
    tables = [ap[f"tbl_{t}"] for t in order]
    dlrm_tower(nc, ap["ids"], ap["ids_picked"], ap["dense"], tables[:K], tables[K:],
               ap["w1"], ap["b1"], ap["w2"], ap["b2"], ap["w3"], out)
    r = run_bass_kernel_spmd(nc, [arrays], core_ids=[0])
    return r.results[0]["out_y_dram"].reshape(B, 1)
```
